# Optimizing a Trainium2 kernel written in Bass

```python
import numpy as np
import jax
import jax.numpy as jnp

def _softmax(x, axis=-1):
    return jax.nn.softmax(x, axis=axis)

def _gelu(x):
    return jax.nn.gelu(x, approximate=True)

def _silu(x):
    return jax.nn.silu(x)

def _sigmoid(x):
    return jax.nn.sigmoid(x)

def _layernorm(x, axis=-1, eps=1e-05):
    m = jnp.mean(x, axis=axis, keepdims=True)
    v = jnp.var(x, axis=axis, keepdims=True)
    return (x - m) / jnp.sqrt(v + eps)

def _scatter_add(tgt, idx, src, axis=0):
    return tgt.at[idx].add(src)

def _segment_sum(src, seg, n):
    return jax.ops.segment_sum(src, seg, n)
kernel_name = 'mk_dlrm_tower_d1_rec_r8_3367c5'

def setup_inputs(seed: int=0):
    np.random.seed(seed)
    _w = jnp.asarray

    def _rec_inputs():
        import jax
        import jax.numpy as jnp
        _tk = jax.random.key(seed)
        dense_ctx = jax.random.normal(jax.random.fold_in(_tk, 190), (2048, 16), jnp.float32)
        ids = jnp.stack([jax.random.randint(jax.random.fold_in(_tk, 200 + f), (2048,), 0, v, jnp.int32) for f, v in enumerate([1250, 12500, 12500, 1000, 1000, 1000, 125000, 1000, 1250, 12500, 12500, 1250, 12500, 1000, 1250, 1250, 1250, 12500, 12500, 1000, 1000, 1000, 1250, 12500, 1250, 1250, 1250, 1250, 1250, 1000, 1250, 1250])], axis=1)
        tbl_0 = 0.05 * jax.random.normal(jax.random.fold_in(_tk, 500 + 0), (1250, 128), jnp.float32)
        tbl_1 = 0.05 * jax.random.normal(jax.random.fold_in(_tk, 500 + 1), (12500, 128), jnp.float32)
        tbl_2 = 0.05 * jax.random.normal(jax.random.fold_in(_tk, 500 + 2), (12500, 128), jnp.float32)
        tbl_3 = 0.05 * jax.random.normal(jax.random.fold_in(_tk, 500 + 3), (1000, 128), jnp.float32)
        tbl_4 = 0.05 * jax.random.normal(jax.random.fold_in(_tk, 500 + 4), (1000, 128), jnp.float32)
        tbl_5 = 0.05 * jax.random.normal(jax.random.fold_in(_tk, 500 + 5), (1000, 128), jnp.float32)
        tbl_6 = 0.05 * jax.random.normal(jax.random.fold_in(_tk, 500 + 6), (125000, 128), jnp.float32)
        tbl_7 = 0.05 * jax.random.normal(jax.random.fold_in(_tk, 500 + 7), (1000, 128), jnp.float32)
        tbl_8 = 0.05 * jax.random.normal(jax.random.fold_in(_tk, 500 + 8), (1250, 128), jnp.float32)
        tbl_9 = 0.05 * jax.random.normal(jax.random.fold_in(_tk, 500 + 9), (12500, 128), jnp.float32)
        tbl_10 = 0.05 * jax.random.normal(jax.random.fold_in(_tk, 500 + 10), (12500, 128), jnp.float32)
        tbl_11 = 0.05 * jax.random.normal(jax.random.fold_in(_tk, 500 + 11), (1250, 128), jnp.float32)
        tbl_12 = 0.05 * jax.random.normal(jax.random.fold_in(_tk, 500 + 12), (12500, 128), jnp.float32)
        tbl_13 = 0.05 * jax.random.normal(jax.random.fold_in(_tk, 500 + 13), (1000, 128), jnp.float32)
        tbl_14 = 0.05 * jax.random.normal(jax.random.fold_in(_tk, 500 + 14), (1250, 128), jnp.float32)
        tbl_15 = 0.05 * jax.random.normal(jax.random.fold_in(_tk, 500 + 15), (1250, 128), jnp.float32)
        tbl_16 = 0.05 * jax.random.normal(jax.random.fold_in(_tk, 500 + 16), (1250, 128), jnp.float32)
        tbl_17 = 0.05 * jax.random.normal(jax.random.fold_in(_tk, 500 + 17), (12500, 128), jnp.float32)
        tbl_18 = 0.05 * jax.random.normal(jax.random.fold_in(_tk, 500 + 18), (12500, 128), jnp.float32)
        tbl_19 = 0.05 * jax.random.normal(jax.random.fold_in(_tk, 500 + 19), (1000, 128), jnp.float32)
        tbl_20 = 0.05 * jax.random.normal(jax.random.fold_in(_tk, 500 + 20), (1000, 128), jnp.float32)
        tbl_21 = 0.05 * jax.random.normal(jax.random.fold_in(_tk, 500 + 21), (1000, 128), jnp.float32)
        tbl_22 = 0.05 * jax.random.normal(jax.random.fold_in(_tk, 500 + 22), (1250, 128), jnp.float32)
        tbl_23 = 0.05 * jax.random.normal(jax.random.fold_in(_tk, 500 + 23), (12500, 128), jnp.float32)
        tbl_24 = 0.05 * jax.random.normal(jax.random.fold_in(_tk, 500 + 24), (1250, 128), jnp.float32)
        tbl_25 = 0.05 * jax.random.normal(jax.random.fold_in(_tk, 500 + 25), (1250, 128), jnp.float32)
        tbl_26 = 0.05 * jax.random.normal(jax.random.fold_in(_tk, 500 + 26), (1250, 128), jnp.float32)
        tbl_27 = 0.05 * jax.random.normal(jax.random.fold_in(_tk, 500 + 27), (1250, 128), jnp.float32)
        tbl_28 = 0.05 * jax.random.normal(jax.random.fold_in(_tk, 500 + 28), (1250, 128), jnp.float32)
        tbl_29 = 0.05 * jax.random.normal(jax.random.fold_in(_tk, 500 + 29), (1000, 128), jnp.float32)
        tbl_30 = 0.05 * jax.random.normal(jax.random.fold_in(_tk, 500 + 30), (1250, 128), jnp.float32)
        tbl_31 = 0.05 * jax.random.normal(jax.random.fold_in(_tk, 500 + 31), (1250, 128), jnp.float32)
        _rk = jax.random.fold_in(_tk, 7)
        W_top1 = 0.0441942 * jax.random.normal(jax.random.fold_in(_tk, 801), (512, 512), jnp.float32)
        W_top2 = 0.0441942 * jax.random.normal(jax.random.fold_in(_tk, 802), (512, 256), jnp.float32)
        W_top3 = 0.0625 * jax.random.normal(jax.random.fold_in(_tk, 803), (256, 1), jnp.float32)
        b_top1 = jnp.zeros((512,), jnp.float32)
        b_top2 = jnp.zeros((256,), jnp.float32)
        return (dense_ctx, ids, tbl_0, tbl_1, tbl_2, tbl_3, tbl_4, tbl_5, tbl_6, tbl_7, tbl_8, tbl_9, tbl_10, tbl_11, tbl_12, tbl_13, tbl_14, tbl_15, tbl_16, tbl_17, tbl_18, tbl_19, tbl_20, tbl_21, tbl_22, tbl_23, tbl_24, tbl_25, tbl_26, tbl_27, tbl_28, tbl_29, tbl_30, tbl_31, W_top1, b_top1, W_top2, b_top2, W_top3)
    dense_ctx, ids, tbl_0, tbl_1, tbl_2, tbl_3, tbl_4, tbl_5, tbl_6, tbl_7, tbl_8, tbl_9, tbl_10, tbl_11, tbl_12, tbl_13, tbl_14, tbl_15, tbl_16, tbl_17, tbl_18, tbl_19, tbl_20, tbl_21, tbl_22, tbl_23, tbl_24, tbl_25, tbl_26, tbl_27, tbl_28, tbl_29, tbl_30, tbl_31, W_top1, b_top1, W_top2, b_top2, W_top3 = _rec_inputs()

    def _L0_rec_setup():
        import jax, jax.numpy as jnp
        import numpy as np
        N_FEATS = 32
        EMBED_D = 128
        BATCH = 2048
        SELF_INTERACTION = False
        key = jax.random.key(seed)
        x = jax.random.normal(key, (BATCH, N_FEATS, EMBED_D), dtype=jnp.float32)
        return {'x': x}
    _L0_rec_all = _L0_rec_setup()
    _L0_rec_in = {k: v for k, v in _L0_rec_all.items() if k in ()}
    del _L0_rec_all
    return {'dense_ctx': dense_ctx, 'ids': ids, 'tbl_0': tbl_0, 'tbl_1': tbl_1, 'tbl_2': tbl_2, 'tbl_3': tbl_3, 'tbl_4': tbl_4, 'tbl_5': tbl_5, 'tbl_6': tbl_6, 'tbl_7': tbl_7, 'tbl_8': tbl_8, 'tbl_9': tbl_9, 'tbl_10': tbl_10, 'tbl_11': tbl_11, 'tbl_12': tbl_12, 'tbl_13': tbl_13, 'tbl_14': tbl_14, 'tbl_15': tbl_15, 'tbl_16': tbl_16, 'tbl_17': tbl_17, 'tbl_18': tbl_18, 'tbl_19': tbl_19, 'tbl_20': tbl_20, 'tbl_21': tbl_21, 'tbl_22': tbl_22, 'tbl_23': tbl_23, 'tbl_24': tbl_24, 'tbl_25': tbl_25, 'tbl_26': tbl_26, 'tbl_27': tbl_27, 'tbl_28': tbl_28, 'tbl_29': tbl_29, 'tbl_30': tbl_30, 'tbl_31': tbl_31, 'W_top1': W_top1, 'b_top1': b_top1, 'W_top2': W_top2, 'b_top2': b_top2, 'W_top3': W_top3}

def reference(dense_ctx, ids, tbl_0, tbl_1, tbl_2, tbl_3, tbl_4, tbl_5, tbl_6, tbl_7, tbl_8, tbl_9, tbl_10, tbl_11, tbl_12, tbl_13, tbl_14, tbl_15, tbl_16, tbl_17, tbl_18, tbl_19, tbl_20, tbl_21, tbl_22, tbl_23, tbl_24, tbl_25, tbl_26, tbl_27, tbl_28, tbl_29, tbl_30, tbl_31, W_top1, b_top1, W_top2, b_top2, W_top3):
    import jax
    import jax.numpy as jnp

    def _L0_rec_ref(x):
        import jax, jax.numpy as jnp
        import numpy as np
        N_FEATS = 32
        EMBED_D = 128
        BATCH = 2048
        SELF_INTERACTION = False
        B, N, D = x.shape
        dot = jnp.einsum('bnd,bmd->bnm', x, x)
        k = 0 if SELF_INTERACTION else 1
        iu, ju = jnp.triu_indices(N, k=k)
        flat = dot[:, iu, ju]
        return flat
    e = jnp.stack([tbl_0[ids[:, 0]], tbl_1[ids[:, 1]], tbl_2[ids[:, 2]], tbl_3[ids[:, 3]], tbl_4[ids[:, 4]], tbl_5[ids[:, 5]], tbl_6[ids[:, 6]], tbl_7[ids[:, 7]], tbl_8[ids[:, 8]], tbl_9[ids[:, 9]], tbl_10[ids[:, 10]], tbl_11[ids[:, 11]], tbl_12[ids[:, 12]], tbl_13[ids[:, 13]], tbl_14[ids[:, 14]], tbl_15[ids[:, 15]], tbl_16[ids[:, 16]], tbl_17[ids[:, 17]], tbl_18[ids[:, 18]], tbl_19[ids[:, 19]], tbl_20[ids[:, 20]], tbl_21[ids[:, 21]], tbl_22[ids[:, 22]], tbl_23[ids[:, 23]], tbl_24[ids[:, 24]], tbl_25[ids[:, 25]], tbl_26[ids[:, 26]], tbl_27[ids[:, 27]], tbl_28[ids[:, 28]], tbl_29[ids[:, 29]], tbl_30[ids[:, 30]], tbl_31[ids[:, 31]]], axis=1)
    z = _L0_rec_ref(e)
    z = z.reshape(z.shape[0], -1)
    h = jnp.concatenate([z, dense_ctx], axis=1)
    h = jnp.maximum(h @ W_top1 + b_top1, 0.0)
    h = jnp.maximum(h @ W_top2 + b_top2, 0.0)
    y = h @ W_top3
    return y

_drawn_inputs = setup_inputs


def setup_inputs(seed=0):
    import zlib

    import numpy as np

    out = dict(_drawn_inputs(seed))
    spreads = {'b_top1': (0.0, 0.1), 'b_top2': (0.0, 0.1)}
    factors = {}
    for name, (base, spread) in spreads.items():
        noise = np.random.default_rng([zlib.crc32(name.encode()), seed]).standard_normal(out[name].shape)
        drawn = base * np.exp(spread * noise) if base else spread * noise
        out[name] = jnp.asarray(drawn.astype(out[name].dtype))
    for name, factor in factors.items():
        out[name] = (out[name] * factor).astype(out[name].dtype)
    return out
```

```python
from contextlib import ExitStack

import concourse.bass as bass
from concourse import mybir

F32 = mybir.dt.float32
I32 = mybir.dt.int32
ALU = mybir.AluOpType
ACT = mybir.ActivationFunctionType

P = 128
BATCH = 2048
FEATS = 32
DENSE = 16
TILES = BATCH // P
BLOCK_TILES = 2
BLOCKS = TILES // BLOCK_TILES
BS = BLOCK_TILES * P
GROUP = 4
GROUPS = FEATS // GROUP
QUADS = 4
QT = P // QUADS
PLANES = FEATS // QUADS
H1 = 512
H2 = 256
C1 = H1 // P
C2 = H2 // P
DMA = 16


def build(nc, ids, row_counts, tables, dense, eye, w1, b1, w2, b2, w3, out):
    with ExitStack() as ctx:
        def sb(name, shape, dt=F32):
            return ctx.enter_context(nc.sbuf_tensor(name, shape, dt))

        def pb(name, shape):
            return ctx.enter_context(nc.psum_tensor(name, shape, F32))

        def sem(name):
            return ctx.enter_context(nc.semaphore(name))

        ids_sb = sb("ids_sb", [P, TILES, FEATS], I32)
        counts_sb = sb("counts_sb", [P, 2, FEATS])
        wrapped = sb("wrapped", [P, TILES, FEATS])
        rows_all = sb("rows_all", [P, TILES, FEATS], I32)
        rows = [sb(f"rows{h}", [P, FEATS], I32) for h in range(2)]
        gathered = sb("gathered", [P, 2, FEATS, P])
        embT = sb("embT", [P, BS, FEATS])
        pairs = sb("pairs", [P, PLANES, BS])
        dense_sb = sb("dense_sb", [P, TILES, FEATS])
        denseT = sb("denseT", [FEATS, TILES, P])
        eye_sb = sb("eye_sb", [P, P])
        w1_sb = sb("w1_sb", [P, PLANES, H1])
        w2_sb = sb("w2_sb", [P, C1, H2])
        w3_sb = sb("w3_sb", [P, C2])
        b1_sb = sb("b1_sb", [P, C1])
        b2_sb = sb("b2_sb", [P, C2])
        h1T = sb("h1T", [P, C1, BS])
        h2T = sb("h2T", [P, C2, BS])
        y_sb = sb("y_sb", [P, TILES])

        dots = pb("dots", [P, QT, FEATS])
        trans = [pb(f"trans{k}", [P, GROUP, P]) for k in range(2)]
        hidden = [pb(f"hidden{k}", [P, H1]) for k in range(2)]
        y_ps = hidden[0][:, BS:BS + BLOCK_TILES]

        ids_loaded = sem("ids_loaded")
        index_step = sem("index_step")
        rows_ready = sem("rows_ready")
        admitted = sem("admitted")
        dense_loaded = sem("dense_loaded")
        weights_loaded = sem("weights_loaded")
        got = [[sem(f"got{h}_{q}") for q in range(GROUPS)] for h in range(2)]
        dense_turned = sem("dense_turned")
        denseT_ready = sem("denseT_ready")
        turned = sem("turned")
        moved = [sem(f"moved{k}") for k in range(2)]
        dotted = sem("dotted")
        pairs_dve = sem("pairs_dve")
        pairs_act = sem("pairs_act")
        layer_out = sem("layer_out")
        relu_done = sem("relu_done")
        y_out = sem("y_out")
        y_moved = sem("y_moved")
        stored = sem("stored")

        def move_dots(copy, h, quads):
            for s in quads:
                for c in range(QUADS):
                    r = 1 if c == 0 else 0
                    inst = copy(
                        pairs[32 * c:32 * c + 32, r:, h * P + s * QT:h * P + (s + 1) * QT].rearrange("p r t -> p t r"),
                        dots[32 * s:32 * s + 32, :, PLANES * c + r:PLANES * (c + 1)])
            return inst

        block = ctx.enter_context(nc.Block())

        @block.sync
        def _(sp):
            sp.dma_start(ids_sb[:], ids.rearrange("(p t) f -> p t f", t=TILES)).then_inc(ids_loaded, DMA)
            sp.dma_start(counts_sb[:], row_counts).then_inc(ids_loaded, DMA)
            sp.dma_start(eye_sb[:], eye).then_inc(dense_loaded, DMA)
            sp.dma_start(dense_sb[:], dense).then_inc(dense_loaded, DMA)
            for dst, src in ((w1_sb, w1), (w2_sb, w2), (w3_sb, w3), (b1_sb, b1), (b2_sb, b2)):
                sp.dma_start(dst[:], src).then_inc(weights_loaded, DMA)
            sp.wait_ge(y_moved, BLOCKS + 1)
            sp.dma_start(out.rearrange("(p t) o -> p (t o)", t=TILES), y_sb[:]).then_inc(stored, DMA)
            sp.wait_ge(stored, DMA)

        @block.gpsimd
        def _(pool):
            def one_block(k, first):
                for h in range(BLOCK_TILES):
                    pool.wait_ge(rows_ready, 2 * k + (h + 1))
                    pool.sem_inc(admitted)
                    for q in range(GROUPS):
                        if not first:
                            pool.wait_ge(turned, 2 * GROUPS * (k - 1) + (GROUPS * h + q + 1))
                            pool.sem_inc(admitted)
                        for f in range(q * GROUP, (q + 1) * GROUP):
                            nc.gpsimd.indirect_dma_start(
                                out=gathered[:, h, f, :], out_offset=None, in_=tables[f],
                                in_offset=bass.IndirectOffsetOnAxis(ap=rows[h][:, f:f + 1], axis=0),
                            ).then_inc(got[h][q], DMA)

            one_block(0, True)
            with pool.Fori(1, BLOCKS) as k:
                one_block(k, False)

        @block.vector
        def _(dve):
            dve.sem_inc(moved[0])
            dve.sem_inc(pairs_dve)
            dve.sem_inc(y_moved)
            dve.wait_ge(ids_loaded, 2 * DMA)
            nrows = counts_sb[:, 0:1, :].broadcast_to([P, TILES, FEATS])
            last = counts_sb[:, 1:2, :].broadcast_to([P, TILES, FEATS])
            nc.vector.scalar_tensor_tensor(wrapped[:], ids_sb[:], 0.0, nrows, ALU.is_lt,
                                           ALU.mult).then_inc(index_step, 1)
            dve.wait_ge(index_step, 1)
            nc.vector.tensor_tensor(wrapped[:], wrapped[:], ids_sb[:], ALU.add).then_inc(index_step, 1)
            dve.wait_ge(index_step, 2)
            nc.vector.scalar_tensor_tensor(rows_all[:], wrapped[:], 0.0, last, ALU.max,
                                           ALU.min).then_inc(index_step, 1)
            dve.wait_ge(index_step, 3)
            for h in range(2):
                nc.vector.tensor_copy(rows[h][:], rows_all[:, h, :]).then_inc(rows_ready, 1)

            def one_block(k, more):
                for h in range(BLOCK_TILES):
                    for q in range(0, GROUPS, 2):
                        dve.wait_ge(turned, 2 * GROUPS * k + (GROUPS * h + q + 1))
                        nc.vector.tensor_copy(
                            embT[:, h * P:(h + 1) * P, q * GROUP:(q + 1) * GROUP].rearrange("p b f -> p f b"),
                            trans[0][:]).then_inc(moved[0], 1)
                    if more:
                        dve.wait_ge(turned, 2 * GROUPS * k + GROUPS * (h + 1))
                        nc.vector.tensor_copy(rows[h][:], rows_all[:, bass.ds(2 * k + (2 + h), 1), :].rearrange(
                            "p o f -> p (o f)")).then_inc(rows_ready, 1)
                    dve.wait_ge(dotted, 2 * k + (h + 1))
                    move_dots(nc.vector.tensor_copy, h, (0, 1)).then_inc(pairs_dve, 1)
                dve.wait_ge(y_out, k + 1)
                nc.vector.tensor_copy(y_sb[:, bass.ds(2 * k, 2)], y_ps).then_inc(y_moved, 1)

            with dve.Fori(0, BLOCKS - 1) as k:
                one_block(k, True)
            one_block(BLOCKS - 1, False)

        @block.scalar
        def _(act):
            act.sem_inc(moved[1])
            act.sem_inc(pairs_act)
            act.wait_ge(dense_turned, 1)
            for s in range(QUADS):
                inst = nc.scalar.copy(denseT[:, s::QUADS, :], trans[0][32 * s:32 * s + 32, :, :])
            inst.then_inc(denseT_ready, 1)
            act.wait_ge(denseT_ready, 1)
            act.wait_ge(weights_loaded, 5 * DMA)

            def one_block(k):
                for h in range(BLOCK_TILES):
                    for q in range(1, GROUPS, 2):
                        act.wait_ge(turned, 2 * GROUPS * k + (GROUPS * h + q + 1))
                        nc.scalar.copy(
                            embT[:, h * P:(h + 1) * P, q * GROUP:(q + 1) * GROUP].rearrange("p b f -> p f b"),
                            trans[1][:]).then_inc(moved[1], 1)
                    act.wait_ge(dotted, 2 * k + (h + 1))
                    nc.scalar.copy(pairs[0:FEATS, 0, h * P:(h + 1) * P],
                                   denseT[:, bass.ds(2 * k + h, 1), :].rearrange("p o b -> p (o b)"))
                    move_dots(nc.scalar.copy, h, (2, 3)).then_inc(pairs_act, 1)
                for u in range(C1 + C2):
                    c, (dst, bias) = (u, (h1T, b1_sb)) if u < C1 else (u - C1, (h2T, b2_sb))
                    act.wait_ge(layer_out, (C1 + C2) * k + (u + 1))
                    nc.scalar.activation(dst[:, c, :], hidden[u % 2][:, 0:BS], ACT.Relu,
                                         bias=bias[:, c:c + 1]).then_inc(relu_done, 1)

            with act.Fori(0, BLOCKS) as k:
                one_block(k)

        @block.tensor
        def _(pe):
            pe.wait_ge(dense_loaded, 2 * DMA)
            for u in range(TILES // QUADS):
                inst = nc.tensor.transpose(trans[0][:, u, :], dense_sb[:, u * QUADS:(u + 1) * QUADS, :].rearrange(
                    "p t f -> p (t f)"), eye_sb[:])
            inst.then_inc(dense_turned, 1)
            pe.wait_ge(denseT_ready, 1)
            pe.wait_ge(weights_loaded, 5 * DMA)

            def one_block(k):
                half = GROUPS // 2
                for h in range(BLOCK_TILES):
                    for q in range(GROUPS):
                        pe.wait_ge(got[h][q], GROUP * DMA * (k + 1))
                        pe.wait_ge(moved[q % 2], GROUPS * k + (half * h + q // 2 + 1))
                        for j in range(GROUP):
                            inst = nc.tensor.transpose(trans[q % 2][:, j, :], gathered[:, h, q * GROUP + j, :],
                                                       eye_sb[:])
                        inst.then_inc(turned, 1)
                    pe.wait_ge(moved[0], GROUPS * k + (half * (h + 1) + 1))
                    pe.wait_ge(moved[1], GROUPS * k + (half * (h + 1) + 1))
                    pe.wait_ge(pairs_dve, 2 * k + (h + 1))
                    pe.wait_ge(pairs_act, 2 * k + (h + 1))
                    for t in range(QT):
                        for s in range(QUADS):
                            e = embT[:, h * P + s * QT + t, :]
                            inst = nc.tensor.matmul(dots[32 * s:32 * s + 32, t, :], e, e, start=True, stop=True)
                    inst.then_inc(dotted, 1)
                pe.wait_ge(pairs_dve, 2 * k + 3)
                pe.wait_ge(pairs_act, 2 * k + 3)
                pe.wait_ge(y_moved, k + 1)
                used = (C1 + C2) * k
                for c in range(C1):
                    if c >= 2:
                        pe.wait_ge(relu_done, used + (c - 1))
                    for r in range(PLANES):
                        inst = nc.tensor.matmul(hidden[c % 2][:, 0:BS], w1_sb[:, r, c * P:(c + 1) * P],
                                                pairs[:, r, :], start=(r == 0), stop=(r == PLANES - 1))
                    inst.then_inc(layer_out, 1)
                pe.wait_ge(relu_done, used + C1)
                for c in range(C2):
                    for r in range(C1):
                        inst = nc.tensor.matmul(hidden[c % 2][:, 0:BS], w2_sb[:, r, c * P:(c + 1) * P],
                                                h1T[:, r, :], start=(r == 0), stop=(r == C1 - 1))
                    inst.then_inc(layer_out, 1)
                pe.wait_ge(relu_done, used + C1 + C2)
                for h in range(BLOCK_TILES):
                    for r in range(C2):
                        inst = nc.tensor.matmul(y_ps[:, h:h + 1], h2T[:, r, h * P:(h + 1) * P], w3_sb[:, r:r + 1],
                                                start=(r == 0), stop=(r == C2 - 1))
                inst.then_inc(y_out, 1)

            with pe.Fori(0, BLOCKS) as k:
                one_block(k)


def pair_rows():
    import numpy as np
    place = np.full((P, PLANES), -1)
    at = 0
    for n in range(FEATS):
        for m in range(n + 1, FEATS):
            place[32 * (m // PLANES) + n, m % PLANES] = at
            at += 1
    place[0:DENSE, 0] = at + np.arange(DENSE)
    return place


def kernel(**inputs):
    import concourse.bacc as bacc
    import numpy as np
    from concourse.bass_utils import run_bass_kernel_spmd

    tables = [np.ascontiguousarray(inputs[f"tbl_{f}"]) for f in range(FEATS)]
    w_top1 = np.asarray(inputs["W_top1"])
    counts = np.array([t.shape[0] for t in tables], np.float32)
    arrays = {
        "ids": np.ascontiguousarray(inputs["ids"]),
        "row_counts": np.ascontiguousarray(np.broadcast_to(np.stack([counts, counts - 1]), (P, 2, FEATS))),
        "dense": np.pad(np.asarray(inputs["dense_ctx"]).reshape(P, TILES, DENSE),
                        ((0, 0), (0, 0), (0, FEATS - DENSE))),
        "eye": np.eye(P, dtype=np.float32),
        "w1": np.ascontiguousarray(np.pad(w_top1, ((0, 1), (0, 0)))[pair_rows()]),
        "b1": np.ascontiguousarray(np.asarray(inputs["b_top1"]).reshape(C1, P).T),
        "w2": np.ascontiguousarray(np.asarray(inputs["W_top2"]).reshape(C1, P, H2).transpose(1, 0, 2)),
        "b2": np.ascontiguousarray(np.asarray(inputs["b_top2"]).reshape(C2, P).T),
        "w3": np.ascontiguousarray(np.asarray(inputs["W_top3"]).reshape(C2, P).T),
    }
    for f, table in enumerate(tables):
        arrays[f"tbl_{f}"] = table

    nc = bacc.Bacc("TRN2", target_bir_lowering=False, num_devices=1)
    ap = {n: nc.dram_tensor(n, a.shape, mybir.dt.from_np(a.dtype), kind="ExternalInput").ap()
          for n, a in arrays.items()}
    out = nc.dram_tensor("y", (BATCH, 1), F32, kind="ExternalOutput").ap()
    build(nc, ap["ids"], ap["row_counts"], [ap[f"tbl_{f}"] for f in range(FEATS)], ap["dense"], ap["eye"],
          ap["w1"], ap["b1"], ap["w2"], ap["b2"], ap["w3"], out)
    return run_bass_kernel_spmd(nc, [arrays], core_ids=[0]).results[0]["y"]
```

```python
from contextlib import ExitStack

import concourse.bass as bass
from concourse import mybir

F32 = mybir.dt.float32
F32R = mybir.dt.float32r
I32 = mybir.dt.int32
ALU = mybir.AluOpType
ACT = mybir.ActivationFunctionType

P = 128
BATCH = 2048
FEATS = 32
DENSE = 16
TILES = BATCH // P
BLOCK_TILES = 2
BLOCKS = TILES // BLOCK_TILES
BS = BLOCK_TILES * P
LAST = BLOCKS - 1
GROUP = 4
LOOKED = (3, 4, 5, 7, 13, 19, 20, 21, 29)
ROWS = 1000
GATHERED = tuple(f for f in range(FEATS) if f not in LOOKED)
ORDER = GATHERED + LOOKED
NG = len(GATHERED)
NL = len(LOOKED)
CHUNKS = 8
RP = ROWS // CHUNKS
RAW = 4
GROUPS = -(-NG // GROUP)
LOOKED_BANKS = -(-NL // 2)
QUADS = 4
QT = P // QUADS
PLANES = FEATS // QUADS
H1 = 512
H2 = 256
C1 = H1 // P
C2 = H2 // P
DMA = 16


def group(g):
    return range(g * GROUP, min((g + 1) * GROUP, NG))


def second_turns(c):
    return range(min(2 * c, GROUPS), min(2 * c + 2, GROUPS))


def build(nc, ids, lookup_ids, row_counts, first_rows, tables, dense, eye, w1, b1, w2, b2, w3, out):
    with ExitStack() as ctx:
        def sb(name, shape, dt=F32):
            return ctx.enter_context(nc.sbuf_tensor(name, shape, dt))

        def pb(name, shape):
            return ctx.enter_context(nc.psum_tensor(name, shape, F32))

        def sem(name):
            return ctx.enter_context(nc.semaphore(name))

        ids_sb = sb("ids_sb", [P, TILES, FEATS], I32)
        counts_sb = sb("counts_sb", [P, 2, FEATS])
        wrapped = sb("wrapped", [P, TILES, FEATS])
        rows_all = sb("rows_all", [P, TILES, FEATS], I32)
        rows = [sb(f"rows{h}", [P, FEATS], I32) for h in range(2)]
        gathered = sb("gathered", [P, 2, NG, P])
        lookup_sb = sb("lookup_sb", [BLOCKS * NL, BS], I32)
        lookup_wrapped = sb("lookup_wrapped", [BLOCKS * NL, BS], I32)
        lookup_row = sb("lookup_row", [BLOCKS * NL, BS])
        lookup_rows = nc.dram_tensor("lookup_rows", (BLOCKS, NL * BS), F32).ap()
        row_sb = sb("row_sb", [P, NL, BS])
        first_rows_sb = sb("first_rows_sb", [P, 1])
        onehot = sb("onehot", [P, 2, CHUNKS, BS], F32R)
        high = sb("high", [P, NL, CHUNKS * P], F32R)
        low = sb("low", [P, NL, CHUNKS * P], F32R)
        embT = sb("embT", [P, BS, FEATS])
        pairs = sb("pairs", [P, PLANES, BS])
        eye_sb = sb("eye_sb", [P, P])
        w1_sb = sb("w1_sb", [P, PLANES, H1])
        raw = w1_sb[0:RP].rearrange("p r n -> p (r n)").rearrange("p (s n) -> p s n", s=RAW)
        w2_sb = sb("w2_sb", [P, C1, H2])
        w3_sb = sb("w3_sb", [P, C2])
        b1_sb = sb("b1_sb", [P, C1])
        b2_sb = sb("b2_sb", [P, C2])
        h1T = sb("h1T", [P, C1, BS])
        h2T = sb("h2T", [P, C2, BS])
        y_sb = sb("y_sb", [P, TILES])

        dots = pb("dots", [P, QT, FEATS])
        trans = [pb(f"trans{k}", [P, GROUP, P]) for k in range(2)]
        hidden = [pb(f"hidden{k}", [P, H1]) for k in range(2)]
        looked = [pb(f"looked{k}", [P, 2, BS]) for k in range(2)]
        y_ps = hidden[0][:, BS:BS + BLOCK_TILES]

        ids_loaded = sem("ids_loaded")
        lookup_ids_loaded = sem("lookup_ids_loaded")
        index_step = sem("index_step")
        rows_ready = sem("rows_ready")
        lookup_step = sem("lookup_step")
        lookup_stored = sem("lookup_stored")
        row_loaded = sem("row_loaded")
        rows_shifted = sem("rows_shifted")
        first_rows_loaded = sem("first_rows_loaded")
        raw_loaded = [sem(f"raw_loaded{k}") for k in range(RAW)]
        high_done = sem("high_done")
        low_done = sem("low_done")
        onehot_ready = sem("onehot_ready")
        lookups = sem("lookups")
        looked_free = sem("looked_free")
        admitted = sem("admitted")
        eye_loaded = sem("eye_loaded")
        dense_in = sem("dense_in")
        weights_loaded = sem("weights_loaded")
        got = [[sem(f"got{h}_{q}") for q in range(GROUPS)] for h in range(2)]
        turned = sem("turned")
        trans_free = sem("trans_free")
        dotted = sem("dotted")
        pairs_dve = sem("pairs_dve")
        pairs_act = sem("pairs_act")
        layer_out = sem("layer_out")
        relu_done = sem("relu_done")
        y_out = sem("y_out")
        y_moved = sem("y_moved")
        stored = sem("stored")

        def move_dots(copy, h, quads):
            for s in quads:
                for c in range(QUADS):
                    r = 1 if c == 0 else 0
                    inst = copy(
                        pairs[32 * c:32 * c + 32, r:, h * P + s * QT:h * P + (s + 1) * QT].rearrange("p r t -> p t r"),
                        dots[32 * s:32 * s + 32, :, PLANES * c + r:PLANES * (c + 1)])
            return inst

        block = ctx.enter_context(nc.Block())

        @block.sync
        def _(sp):
            sp.dma_start(ids_sb[:], ids.rearrange("(p t) f -> p t f", t=TILES)).then_inc(ids_loaded, DMA)
            sp.dma_start(lookup_sb[:], lookup_ids).then_inc(lookup_ids_loaded, DMA)
            for j, f in enumerate(LOOKED):
                if j >= RAW:
                    sp.wait_ge(low_done, j - RAW + 1)
                src = tables[f].rearrange("(p c) d -> p (c d)", c=CHUNKS)
                for p0, p1 in ((0, RP // 16 * 16), (RP // 16 * 16, RP)):
                    sp.dma_start(raw[p0:p1, j % RAW, :], src[p0:p1, :]).then_inc(raw_loaded[j % RAW], DMA)
                if j == 1:
                    sp.wait_ge(lookup_step, 3)
                    sp.dma_start(lookup_rows.rearrange("k (j b) -> (k j) b", j=NL),
                                 lookup_row[:]).then_inc(lookup_stored, DMA)
                if j == 3:
                    sp.wait_ge(lookup_stored, DMA)
                    sp.dma_start(row_sb[:], lookup_rows[0:1, :].broadcast_to([P, NL * BS]).rearrange(
                        "p (j b) -> p j b", j=NL)).then_inc(row_loaded, DMA)
            sp.wait_ge(low_done, NL)
            for dst, src in ((w1_sb, w1), (w2_sb, w2), (w3_sb, w3), (b1_sb, b1), (b2_sb, b2)):
                sp.dma_start(dst[:], src).then_inc(weights_loaded, DMA)

            def load_dense(k):
                sp.wait_ge(dotted, 2 * k + 1)
                sp.dma_start(pairs[0:FEATS, 0:1, :], dense[bass.ds(k, 1), :, :].rearrange(
                    "o f b -> f o b")).then_inc(dense_in, DMA)

            with sp.Fori(0, LAST) as k:
                sp.wait_ge(onehot_ready, NL * (k + 1))
                sp.dma_start(row_sb[:], lookup_rows[bass.ds(k + 1, 1), :].broadcast_to([P, NL * BS]).rearrange(
                    "p (j b) -> p j b", j=NL)).then_inc(row_loaded, DMA)
                load_dense(k)
            load_dense(LAST)
            sp.wait_ge(y_moved, LAST + 3)
            sp.dma_start(out.rearrange("(p t) o -> p (t o)", t=TILES), y_sb[:]).then_inc(stored, DMA)
            sp.wait_ge(stored, DMA)

        @block.gpsimd
        def _(pool):
            pool.wait_ge(lookup_ids_loaded, DMA)
            nc.gpsimd.tensor_scalar(lookup_wrapped[:], lookup_sb[:], 0.0, float(ROWS), ALU.is_lt,
                                    ALU.mult).then_inc(lookup_step, 1)
            pool.wait_ge(lookup_step, 1)
            nc.gpsimd.tensor_tensor(lookup_wrapped[:], lookup_wrapped[:], lookup_sb[:],
                                    ALU.add).then_inc(lookup_step, 1)
            pool.wait_ge(lookup_step, 2)
            nc.gpsimd.tensor_scalar(lookup_row[:], lookup_wrapped[:], 0.0, float(ROWS - 1), ALU.max,
                                    ALU.min).then_inc(lookup_step, 1)

            def one_block(k, first):
                for h in range(BLOCK_TILES):
                    pool.wait_ge(rows_ready, 2 * k + (h + 1))
                    pool.sem_inc(admitted)
                    for q in range(GROUPS):
                        if not first:
                            pool.wait_ge(turned, 2 * GROUPS * (k - 1) + (GROUPS * h + q + 1))
                            pool.sem_inc(admitted)
                        for g in group(q):
                            f = GATHERED[g]
                            nc.gpsimd.indirect_dma_start(
                                out=gathered[:, h, g, :], out_offset=None, in_=tables[f],
                                in_offset=bass.IndirectOffsetOnAxis(ap=rows[h][:, f:f + 1], axis=0),
                            ).then_inc(got[h][q], DMA)

            one_block(0, True)
            with pool.Fori(1, BLOCKS) as k:
                one_block(k, False)

        @block.vector
        def _(dve):
            dve.sem_inc(pairs_dve)
            dve.sem_inc(y_moved)
            dve.wait_ge(ids_loaded, 2 * DMA)
            step = 0
            for t0, t1 in ((0, 2), (2, TILES)):
                nrows, last = (counts_sb[:, n:n + 1, :].broadcast_to([P, t1 - t0, FEATS]) for n in range(2))
                nc.vector.scalar_tensor_tensor(wrapped[:, t0:t1], ids_sb[:, t0:t1], 0.0, nrows, ALU.is_lt,
                                               ALU.mult).then_inc(index_step, 1)
                dve.wait_ge(index_step, step + 1)
                nc.vector.tensor_tensor(wrapped[:, t0:t1], wrapped[:, t0:t1], ids_sb[:, t0:t1],
                                        ALU.add).then_inc(index_step, 1)
                dve.wait_ge(index_step, step + 2)
                nc.vector.scalar_tensor_tensor(rows_all[:, t0:t1], wrapped[:, t0:t1], 0.0, last, ALU.max,
                                               ALU.min).then_inc(index_step, 1)
                dve.wait_ge(index_step, step + 3)
                step += 3
                if t0 == 0:
                    for h in range(2):
                        nc.vector.tensor_copy(rows[h][:], rows_all[:, h, :]).then_inc(rows_ready, 1)
            for j in range(NL):
                dve.wait_ge(high_done, j + 1)
                nc.vector.tensor_tensor(low[0:RP, j, :], raw[:, j % RAW, :], high[0:RP, j, :].bitcast(F32),
                                        ALU.subtract).then_inc(low_done, 1)

            def make_onehot(j):
                for c in range(CHUNKS):
                    inst = nc.vector.tensor_scalar(onehot[0:RP, j % 2, c, :], row_sb[0:RP, j, :],
                                                   float(c), None, ALU.is_equal)
                inst.then_inc(onehot_ready, 1)

            def next_rows(k, h):
                dve.wait_ge(turned, 2 * GROUPS * k + GROUPS * (h + 1))
                nc.vector.tensor_copy(rows[h][:], rows_all[:, bass.ds(2 * k + (2 + h), 1), :].rearrange(
                    "p o f -> p (o f)")).then_inc(rows_ready, 1)

            def other_onehots(k):
                for j in range(2, NL):
                    dve.wait_ge(lookups, NL * k + (j - 1))
                    make_onehot(j)

            def first_onehots(k):
                dve.wait_ge(row_loaded, DMA * (k + 1))
                nc.vector.tensor_scalar(row_sb[:], row_sb[:], first_rows_sb[:, 0:1], None,
                                        ALU.subtract).then_inc(rows_shifted, 1)
                dve.wait_ge(rows_shifted, k + 1)
                make_onehot(0)
                make_onehot(1)

            def move_dots_of(k, h):
                dve.wait_ge(dotted, 2 * k + (h + 1))
                move_dots(nc.vector.tensor_copy, h, (0, 1)).then_inc(pairs_dve, 1)

            def move_results(rnd, first, n):
                dve.wait_ge(y_out, rnd + 1)
                nc.vector.tensor_copy(y_sb[:, bass.ds(first, n)], y_ps[:, 0:n]).then_inc(y_moved, 1)

            dve.wait_ge(first_rows_loaded, DMA)
            first_onehots(0)
            other_onehots(0)
            next_rows(0, 0)
            next_rows(0, 1)
            move_dots_of(0, 0)
            first_onehots(1)
            move_dots_of(0, 1)
            with dve.Fori(1, LAST) as k:
                other_onehots(k)
                next_rows(k, 0)
                next_rows(k, 1)
                move_dots_of(k, 0)
                first_onehots(k + 1)
                move_dots_of(k, 1)
                move_results(k - 1, 2 * (k - 1), 2)
            other_onehots(LAST)
            move_dots_of(LAST, 0)
            move_results(LAST - 1, 2 * (LAST - 1), 2)
            move_results(LAST, TILES - 2, 1)
            move_dots_of(LAST, 1)
            move_results(LAST + 1, TILES - 1, 1)

        @block.scalar
        def _(act):
            act.dma_start(counts_sb[:], row_counts).then_inc(ids_loaded, DMA)
            act.dma_start(first_rows_sb[:], first_rows).then_inc(first_rows_loaded, DMA)
            act.dma_start(eye_sb[:], eye).then_inc(eye_loaded, DMA)
            act.sem_inc(pairs_act)
            act.sem_inc(trans_free, 2)
            act.sem_inc(looked_free, 2)
            for j in range(NL):
                act.wait_ge(raw_loaded[j % RAW], 2 * DMA * (j // RAW + 1))
                nc.scalar.copy(high[0:RP, j, :], raw[:, j % RAW, :]).then_inc(high_done, 1)

            def move_turned(k, h, g):
                act.wait_ge(turned, 2 * GROUPS * k + (GROUPS * h + g + 1))
                places = group(g)
                nc.scalar.copy(
                    embT[:, h * P:(h + 1) * P, places[0]:places[-1] + 1].rearrange("p b f -> p f b"),
                    trans[g % 2][:, 0:len(places), :]).then_inc(trans_free, 1)

            def lookups_and_turns(k):
                for j in range(NL):
                    if j % 2 == 1 or j == NL - 1:
                        first = j // 2 * 2
                        act.wait_ge(lookups, NL * k + (j + 1))
                        nc.scalar.copy(embT[:, :, NG + first:NG + j + 1].rearrange("p b f -> p f b"),
                                       looked[j // 2 % 2][:, 0:j + 1 - first, :]).then_inc(looked_free, 1)
                    if j < GROUPS:
                        move_turned(k, 0, j)

            def relu(rnd, u, cols=slice(0, BS)):
                c, (dst, bias) = (u, (h1T, b1_sb)) if u < C1 else (u - C1, (h2T, b2_sb))
                act.wait_ge(layer_out, (C1 + C2) * rnd + (u + 1))
                nc.scalar.activation(dst[:, c, cols], hidden[u % 2][:, cols], ACT.Relu,
                                     bias=bias[:, c:c + 1]).then_inc(relu_done, 1)

            def move_dots_of(k, h):
                act.wait_ge(dotted, 2 * k + (h + 1))
                move_dots(nc.scalar.copy, h, (2, 3)).then_inc(pairs_act, 1)

            lookups_and_turns(0)
            for g in range(GROUPS):
                move_turned(0, 1, g)
            act.wait_ge(weights_loaded, 5 * DMA)
            move_dots_of(0, 0)
            move_dots_of(0, 1)
            with act.Fori(1, LAST) as k:
                lookups_and_turns(k)
                for c in range(C1):
                    for g in second_turns(c):
                        move_turned(k, 1, g)
                    relu(k - 1, c)
                move_dots_of(k, 0)
                for c in range(C2):
                    relu(k - 1, C1 + c)
                move_dots_of(k, 1)
            lookups_and_turns(LAST)
            for c in range(C1):
                relu(LAST - 1, c)
            move_dots_of(LAST, 0)
            for c in range(C2):
                relu(LAST - 1, C1 + c)
            for u in range(C1 + C2):
                relu(LAST, u, slice(0, P))
            for g in range(GROUPS):
                move_turned(LAST, 1, g)
            move_dots_of(LAST, 1)
            for u in range(C1 + C2):
                relu(LAST + 1, u, slice(P, BS))

        @block.tensor
        def _(pe):
            pe.wait_ge(eye_loaded, DMA)

            def look_up(k, j):
                bank, half = j // 2 % 2, j % 2
                if half == 0:
                    pe.wait_ge(looked_free, LOOKED_BANKS * k + (j // 2 + 1 + (LOOKED_BANKS % 2 if j == 0 else 0)))
                pe.wait_ge(onehot_ready, NL * k + (j + 1))
                for c in range(CHUNKS):
                    for part in (high, low):
                        inst = nc.tensor.matmul(looked[bank][:, half, :], part[0:RP, j, c * P:(c + 1) * P],
                                                onehot[0:RP, j % 2, c, :], start=(c == 0 and part is high),
                                                stop=(c == CHUNKS - 1 and part is low))
                inst.then_inc(lookups, 1)

            def turn(k, h, g):
                pe.wait_ge(got[h][g], len(group(g)) * DMA * (k + 1))
                pe.wait_ge(trans_free, 2 * GROUPS * k + (GROUPS * h + g + 1))
                for j, place in enumerate(group(g)):
                    inst = nc.tensor.transpose(trans[g % 2][:, j, :], gathered[:, h, place, :], eye_sb[:])
                inst.then_inc(turned, 1)

            def dot(k, h):
                pe.wait_ge(looked_free, LOOKED_BANKS * k + (LOOKED_BANKS + 2))
                pe.wait_ge(trans_free, 2 * GROUPS * k + (GROUPS * (h + 1) + 2))
                pe.wait_ge(pairs_dve, 2 * k + (h + 1))
                pe.wait_ge(pairs_act, 2 * k + (h + 1))
                for t in range(QT):
                    for s in range(QUADS):
                        e = embT[:, h * P + s * QT + t, :]
                        inst = nc.tensor.matmul(dots[32 * s:32 * s + 32, t, :], e, e, start=True, stop=True)
                inst.then_inc(dotted, 1)

            def layer1(rnd, c, turns=(), cols=slice(0, BS)):
                turns = list(turns)
                if c == 0:
                    pe.wait_ge(y_moved, rnd + 1)
                if c >= 2:
                    pe.wait_ge(relu_done, (C1 + C2) * rnd + (c - 1))
                for r in range(PLANES):
                    inst = nc.tensor.matmul(hidden[c % 2][:, cols], w1_sb[:, r, c * P:(c + 1) * P],
                                            pairs[:, r, cols], start=(r == 0), stop=(r == PLANES - 1))
                    if r == PLANES - 1:
                        inst.then_inc(layer_out, 1)
                    if turns and r in (PLANES // 2 - 1, PLANES - 1):
                        turn(*turns.pop(0))

            def layer2(rnd, cols=slice(0, BS)):
                pe.wait_ge(relu_done, (C1 + C2) * rnd + C1)
                for c in range(C2):
                    for r in range(C1):
                        inst = nc.tensor.matmul(hidden[c % 2][:, cols], w2_sb[:, r, c * P:(c + 1) * P],
                                                h1T[:, r, cols], start=(r == 0), stop=(r == C1 - 1))
                    inst.then_inc(layer_out, 1)

            def layer3(rnd, tiles=(0, 1)):
                pe.wait_ge(relu_done, (C1 + C2) * (rnd + 1))
                for n, h in enumerate(tiles):
                    for r in range(C2):
                        inst = nc.tensor.matmul(y_ps[:, n:n + 1], h2T[:, r, h * P:(h + 1) * P], w3_sb[:, r:r + 1],
                                                start=(r == 0), stop=(r == C2 - 1))
                inst.then_inc(y_out, 1)

            def wait_pairs(tiles, blocks):
                pe.wait_ge(pairs_dve, tiles + 1)
                pe.wait_ge(pairs_act, tiles + 1)
                pe.wait_ge(dense_in, DMA * blocks)

            for j in range(NL):
                pe.wait_ge(low_done, j + 1)
                look_up(0, j)
                if j < GROUPS:
                    turn(0, 0, j)
            for g in range(GROUPS):
                turn(0, 1, g)
            dot(0, 0)
            dot(0, 1)
            pe.wait_ge(weights_loaded, 5 * DMA)
            with pe.Fori(1, LAST) as k:
                for j in range(NL):
                    look_up(k, j)
                    if j < GROUPS:
                        turn(k, 0, j)
                wait_pairs(2 * k, k)
                for c in range(C1):
                    layer1(k - 1, c, [(k, 1, g) for g in second_turns(c)])
                dot(k, 0)
                layer2(k - 1)
                dot(k, 1)
                layer3(k - 1)
            for j in range(NL):
                look_up(LAST, j)
                if j < GROUPS:
                    turn(LAST, 0, j)
            wait_pairs(2 * LAST, LAST)
            for c in range(C1):
                layer1(LAST - 1, c)
            dot(LAST, 0)
            layer2(LAST - 1)
            layer3(LAST - 1)
            wait_pairs(TILES - 1, BLOCKS)
            for c in range(C1):
                layer1(LAST, c, cols=slice(0, P))
            layer2(LAST, slice(0, P))
            layer3(LAST, (0,))
            for g in range(GROUPS):
                turn(LAST, 1, g)
            dot(LAST, 1)
            wait_pairs(TILES, BLOCKS)
            for c in range(C1):
                layer1(LAST + 1, c, cols=slice(P, BS))
            layer2(LAST + 1, slice(P, BS))
            layer3(LAST + 1, (1,))


def pair_rows():
    import numpy as np
    place = np.full((P, PLANES), -1)
    where = {f: n for n, f in enumerate(ORDER)}
    at = 0
    for a in range(FEATS):
        for b in range(a + 1, FEATS):
            n, m = sorted((where[a], where[b]))
            place[32 * (m // PLANES) + n, m % PLANES] = at
            at += 1
    place[0:DENSE, 0] = at + np.arange(DENSE)
    return place


def kernel(**inputs):
    import concourse.bacc as bacc
    import numpy as np
    from concourse.bass_utils import run_bass_kernel_spmd

    tables = [np.ascontiguousarray(inputs[f"tbl_{f}"]) for f in range(FEATS)]
    w_top1 = np.asarray(inputs["W_top1"])
    counts = np.array([t.shape[0] for t in tables], np.float32)
    arrays = {
        "ids": np.ascontiguousarray(inputs["ids"]),
        "lookup_ids": np.ascontiguousarray(
            np.asarray(inputs["ids"])[:, LOOKED].reshape(P, BLOCKS, BLOCK_TILES, NL).transpose(1, 3, 2, 0)
        ).reshape(BLOCKS * NL, BS),
        "first_rows": CHUNKS * np.arange(P, dtype=np.float32)[:, None],
        "row_counts": np.ascontiguousarray(np.broadcast_to(np.stack([counts, counts - 1]), (P, 2, FEATS))),
        "dense": np.ascontiguousarray(np.pad(
            np.asarray(inputs["dense_ctx"]).reshape(P, BLOCKS, BLOCK_TILES, DENSE).transpose(1, 3, 2, 0),
            ((0, 0), (0, FEATS - DENSE), (0, 0), (0, 0))).reshape(BLOCKS, FEATS, BS)),
        "eye": np.eye(P, dtype=np.float32),
        "w1": np.ascontiguousarray(np.pad(w_top1, ((0, 1), (0, 0)))[pair_rows()]),
        "b1": np.ascontiguousarray(np.asarray(inputs["b_top1"]).reshape(C1, P).T),
        "w2": np.ascontiguousarray(np.asarray(inputs["W_top2"]).reshape(C1, P, H2).transpose(1, 0, 2)),
        "b2": np.ascontiguousarray(np.asarray(inputs["b_top2"]).reshape(C2, P).T),
        "w3": np.ascontiguousarray(np.asarray(inputs["W_top3"]).reshape(C2, P).T),
    }
    for f, table in enumerate(tables):
        arrays[f"tbl_{f}"] = table

    nc = bacc.Bacc("TRN2", target_bir_lowering=False, num_devices=1)
    ap = {n: nc.dram_tensor(n, a.shape, mybir.dt.from_np(a.dtype), kind="ExternalInput").ap()
          for n, a in arrays.items()}
    out = nc.dram_tensor("y", (BATCH, 1), F32, kind="ExternalOutput").ap()
    build(nc, ap["ids"], ap["lookup_ids"], ap["row_counts"], ap["first_rows"], [ap[f"tbl_{f}"] for f in range(FEATS)], ap["dense"], ap["eye"],
          ap["w1"], ap["b1"], ap["w2"], ap["b2"], ap["w3"], out)
    return run_bass_kernel_spmd(nc, [arrays], core_ids=[0]).results[0]["y"]
```

```python
from contextlib import ExitStack

import concourse.bass as bass
from concourse import mybir

F32 = mybir.dt.float32
F16 = mybir.dt.float16
F32R = mybir.dt.float32r
I32 = mybir.dt.int32
ALU = mybir.AluOpType
ACT = mybir.ActivationFunctionType

P = 128
BATCH = 2048
FEATS = 32
DENSE = 16
TILES = BATCH // P
BLOCK_TILES = 2
BLOCKS = TILES // BLOCK_TILES
BS = BLOCK_TILES * P
LAST = BLOCKS - 1
FIRST_TILE = slice(0, P)
SECOND_TILE = slice(P, BS)
GROUP = 4
LOOKED = (3, 4, 5, 7, 13, 19, 20, 21, 29, 0)
LOOKED_ROWS = (1000,) * 9 + (1250,)
RP = 125
CHUNKS = tuple(n // RP for n in LOOKED_ROWS)
MAX_CHUNKS = max(CHUNKS)
GATHERED = tuple(f for f in range(FEATS) if f not in LOOKED)
ORDER = GATHERED + LOOKED
NG = len(GATHERED)
NL = len(LOOKED)
RING = 3
RAW = 3
FIRST_TURNS = 4
GROUPS = -(-NG // GROUP)
EARLY_ONEHOTS = RING + 4
CHUNK_AT = [sum(CHUNKS[:j]) for j in range(NL + 1)]
SLOT_CHUNKS = [max(CHUNKS[j::RING]) for j in range(RING)]
SLOT_AT = [sum(SLOT_CHUNKS[:j]) for j in range(RING + 1)]
ALIKE = [(j, j + CHUNKS.count(CHUNKS[j])) for j in range(NL) if j == 0 or CHUNKS[j] != CHUNKS[j - 1]]
assert NL % 2 == 0
LOOKED_BANKS = NL // 2
QUADS = 4
QT = P // QUADS
PLANES = 5
LAYOUT = (
    ((0, 32, 0, 5), (1, 32, 5, 5), (2, 32, 10, 5), (3, 32, 30, 2)),
    ((0, 20, 15, 5), (1, 25, 20, 5), (2, 30, 25, 5), (3, 15, 10, 5)),
    ((1, 5, 0, 5), (2, 10, 5, 5)),
)
UNDER = len(LAYOUT) - 1
DENSE_ROW = 25
DENSE_PLANE = 2
DENSE_PLANES = PLANES - DENSE_PLANE
H1 = 512
H2 = 256
C1 = H1 // P
C2 = H2 // P
SECOND_TURNS = C1 - (GROUPS - FIRST_TURNS)
assert SECOND_TURNS + 4 == GROUPS
DMA = 16


def group(g):
    return range(g * GROUP, min((g + 1) * GROUP, NG))


def turns_after_lookup(j):
    return [j // 2] if j % 2 == 1 and j // 2 < FIRST_TURNS else []


def turns_after_chunk(c):
    return ((0, FIRST_TURNS + c),) if FIRST_TURNS + c < GROUPS else ((1, FIRST_TURNS + c - GROUPS),)


def build(nc, ids, lookup_ids, lookup_counts, row_counts, first_rows, tables, dense, eye, w1, b1, w2, b2, w3, out):
    with ExitStack() as ctx:
        def sb(name, shape, dt=F32):
            return ctx.enter_context(nc.sbuf_tensor(name, shape, dt))

        def pb(name, shape):
            return ctx.enter_context(nc.psum_tensor(name, shape, F32))

        def sem(name):
            return ctx.enter_context(nc.semaphore(name))

        ids_sb = sb("ids_sb", [P, TILES, FEATS], I32)
        counts_sb = sb("counts_sb", [P, 2, FEATS])
        rows_all = sb("rows_all", [P, TILES, FEATS], I32)
        rows = [sb(f"rows{h}", [P, FEATS], I32) for h in range(2)]
        gathered = sb("gathered", [P, 2, NG, P])
        lookup_counts_sb = sb("lookup_counts_sb", [BLOCKS * NL, 2])
        lookup_row = sb("lookup_row", [BLOCKS * NL, BS], F16)
        lookup_rows = nc.dram_tensor("lookup_rows", (BLOCKS, NL * BS), F16).ap()
        row_sb = sb("row_sb", [P, NL, BS], F16)
        first_rows_sb = sb("first_rows_sb", [P, len(ALIKE)])
        onehot = sb("onehot", [P, SLOT_AT[RING], BS], F32R)
        high = sb("high", [P, CHUNK_AT[NL] * P], F32R)
        low = sb("low", [P, CHUNK_AT[NL] * P], F32R)
        embT = sb("embT", [P, BS, FEATS])
        pairs = sb("pairs", [P, PLANES, BS])
        lookup_sb = pairs[0:BLOCKS * NL, 0, :].bitcast(I32)
        lookup_wrapped = pairs[0:BLOCKS * NL, 1, :]
        wrapped = pairs[:, 2:4, :].rearrange("p r b -> p (r b)").rearrange("p (t f) -> p t f", f=FEATS)
        eye_sb = sb("eye_sb", [P, P])
        w1_place = sb("w1_place", [P, RAW * MAX_CHUNKS * P])
        w1_sb = w1_place[:, 0:PLANES * H1].rearrange("p (r n) -> p r n", r=PLANES)
        raw = w1_place[0:RP].rearrange("p (s n) -> p s n", s=RAW)
        w2_sb = sb("w2_sb", [P, C1, H2])
        w3_sb = sb("w3_sb", [P, C2])
        b1_sb = sb("b1_sb", [P, C1])
        b2_sb = sb("b2_sb", [P, C2])
        h1T = sb("h1T", [P, C1, BS])
        h2T = sb("h2T", [P, C2, BS])
        y_sb = sb("y_sb", [P, TILES])

        dots = pb("dots", [P, QT, FEATS])
        trans = [pb(f"trans{k}", [P, GROUP, P]) for k in range(2)]
        hidden = [pb(f"hidden{k}", [P, H1]) for k in range(2)]
        looked = [pb(f"looked{k}", [P, 2, BS]) for k in range(2)]
        y_ps = hidden[0][:, BS:BS + BLOCK_TILES]
        last_y_ps = looked[0][:, 0, 0:BLOCK_TILES]

        ids_loaded = sem("ids_loaded")
        lookup_ids_loaded = sem("lookup_ids_loaded")
        index_step = sem("index_step")
        rows_ready = sem("rows_ready")
        lookup_step = sem("lookup_step")
        lookup_stored = sem("lookup_stored")
        row_loaded = sem("row_loaded")
        rows_shifted = sem("rows_shifted")
        first_rows_loaded = sem("first_rows_loaded")
        raw_loaded = [sem(f"raw_loaded{k}") for k in range(RAW)]
        high_done = sem("high_done")
        low_done = sem("low_done")
        onehot_ready = sem("onehot_ready")
        lookups = sem("lookups")
        looked_free = sem("looked_free")
        admitted = sem("admitted")
        eye_loaded = sem("eye_loaded")
        dense_in = sem("dense_in")
        weights_loaded = sem("weights_loaded")
        got = [[sem(f"got{h}_{q}") for q in range(GROUPS)] for h in range(2)]
        turned = sem("turned")
        trans_free = sem("trans_free")
        dotted = sem("dotted")
        under_dve = sem("under_dve")
        under_act = sem("under_act")
        half_dotted = sem("half_dotted")
        pairs_dve = sem("pairs_dve")
        pairs_act = sem("pairs_act")
        layer_out = sem("layer_out")
        relu_done = sem("relu_done")
        y_out = sem("y_out")
        y_moved = sem("y_moved")
        stored = sem("stored")

        def move_dots(copy, h, s, step, t0=0, t1=QT):
            first = h * P + s * QT
            for c, n, m, cols in step:
                inst = copy(pairs[32 * c:32 * c + n, 0:cols, first + t0:first + t1].rearrange("p r t -> p t r"),
                            dots[32 * s:32 * s + n, t0:t1, m:m + cols])
            return inst

        block = ctx.enter_context(nc.Block())

        @block.sync
        def _(sp):
            sp.dma_start(ids_sb[:], ids.rearrange("(p t) f -> p t f", t=TILES)).then_inc(ids_loaded, DMA)
            sp.dma_start(lookup_sb, lookup_ids).then_inc(lookup_ids_loaded, DMA)
            for j, f in enumerate(LOOKED):
                if j >= RAW:
                    sp.wait_ge(low_done, j - RAW + 1)
                src = tables[f].rearrange("(p c) d -> p (c d)", c=CHUNKS[j])
                for p0, p1 in ((0, RP // 16 * 16), (RP // 16 * 16, RP)):
                    sp.dma_start(raw[p0:p1, j % RAW, 0:CHUNKS[j] * P], src[p0:p1, :]).then_inc(raw_loaded[j % RAW], DMA)
            sp.wait_ge(low_done, NL)
            for dst, src in ((w1_sb, w1), (w2_sb[:], w2), (w3_sb[:], w3), (b1_sb[:], b1), (b2_sb[:], b2)):
                sp.dma_start(dst, src).then_inc(weights_loaded, DMA)

            def load_dense(k):
                sp.wait_ge(dotted, 2 * k + 1)
                sp.dma_start(pairs[96 + DENSE_ROW:P, DENSE_PLANE:, :],
                             dense[bass.ds(k, 1), :, :, :].rearrange("o n r b -> (o n) r b")).then_inc(dense_in, DMA)

            with sp.Fori(0, LAST) as k:
                sp.wait_ge(onehot_ready, NL * (k + 1))
                sp.dma_start(row_sb[:], lookup_rows[bass.ds(k + 1, 1), :].broadcast_to([P, NL * BS]).rearrange(
                    "p (j b) -> p j b", j=NL)).then_inc(row_loaded, DMA)
                load_dense(k)
            load_dense(LAST)
            sp.wait_ge(y_moved, BLOCKS + 1)
            sp.dma_start(out.rearrange("(p t) o -> p (t o)", t=TILES), y_sb[:]).then_inc(stored, DMA)
            sp.wait_ge(stored, DMA)

        @block.gpsimd
        def _(pool):
            def one_block(k, first):
                for h in range(BLOCK_TILES):
                    pool.wait_ge(rows_ready, 2 * k + (h + 1))
                    pool.sem_inc(admitted)
                    for q in range(GROUPS):
                        if not first:
                            pool.wait_ge(turned, 2 * GROUPS * (k - 1) + (GROUPS * h + q + 1))
                            pool.sem_inc(admitted)
                        for g in group(q):
                            f = GATHERED[g]
                            nc.gpsimd.indirect_dma_start(
                                out=gathered[:, h, g, :], out_offset=None, in_=tables[f],
                                in_offset=bass.IndirectOffsetOnAxis(ap=rows[h][:, f:f + 1], axis=0),
                            ).then_inc(got[h][q], DMA)

            one_block(0, True)
            with pool.Fori(1, BLOCKS) as k:
                one_block(k, False)

        @block.vector
        def _(dve):
            dve.sem_inc(y_moved)

            def tile_rows(step, t0, t1):
                nrows, last = (counts_sb[:, n:n + 1, :].broadcast_to([P, t1 - t0, FEATS]) for n in range(2))
                nc.vector.scalar_tensor_tensor(wrapped[:, t0:t1], ids_sb[:, t0:t1], 0.0, nrows, ALU.is_lt,
                                               ALU.mult).then_inc(index_step, 1)
                dve.wait_ge(index_step, step + 1)
                nc.vector.tensor_tensor(wrapped[:, t0:t1], wrapped[:, t0:t1], ids_sb[:, t0:t1],
                                        ALU.add).then_inc(index_step, 1)
                dve.wait_ge(index_step, step + 2)
                nc.vector.scalar_tensor_tensor(rows_all[:, t0:t1], wrapped[:, t0:t1], 0.0, last, ALU.max,
                                               ALU.min).then_inc(index_step, 1)
                dve.wait_ge(index_step, step + 3)

            dve.wait_ge(ids_loaded, 2 * DMA)
            tile_rows(0, 0, BLOCK_TILES)
            for h in range(2):
                nc.vector.tensor_copy(rows[h][:], rows_all[:, h, :]).then_inc(rows_ready, 1)
            dve.wait_ge(lookup_ids_loaded, 2 * DMA)
            nc.vector.tensor_scalar(lookup_wrapped, lookup_sb, 0.0, lookup_counts_sb[:, 0:1], ALU.is_lt,
                                    ALU.mult).then_inc(lookup_step, 1)
            dve.wait_ge(lookup_step, 1)
            nc.vector.tensor_tensor(lookup_wrapped, lookup_wrapped, lookup_sb, ALU.add).then_inc(lookup_step, 1)
            dve.wait_ge(lookup_step, 2)
            nc.vector.tensor_scalar(lookup_row[:], lookup_wrapped, 0.0, lookup_counts_sb[:, 1:2], ALU.max,
                                    ALU.min).then_inc(lookup_step, 1)
            tile_rows(3, BLOCK_TILES, TILES)
            dve.wait_ge(lookup_step, 3)
            nc.vector.memset(pairs[96:P, DENSE_PLANE:, :], 0.0).then_inc(pairs_dve, 1)

            def split_low(j):
                dve.wait_ge(high_done, j + 1)
                part = slice(CHUNK_AT[j] * P, CHUNK_AT[j + 1] * P)
                nc.vector.tensor_tensor(low[0:RP, part], raw[:, j % RAW, 0:CHUNKS[j] * P],
                                        high[0:RP, part].bitcast(F32), ALU.subtract).then_inc(low_done, 1)

            def make_onehot(j):
                for c in range(CHUNKS[j]):
                    inst = nc.vector.tensor_scalar(onehot[0:RP, SLOT_AT[j % RING] + c, :], row_sb[0:RP, j, :],
                                                   float(c), None, ALU.is_equal)
                inst.then_inc(onehot_ready, 1)

            def next_rows(k, h):
                for q in range(GROUPS):
                    dve.wait_ge(got[h][q], len(group(q)) * DMA * (k + 1))
                nc.vector.tensor_copy(rows[h][:], rows_all[:, bass.ds(2 * k + (2 + h), 1), :].rearrange(
                    "p o f -> p (o f)")).then_inc(rows_ready, 1)

            def other_onehots(k):
                for j in range(EARLY_ONEHOTS, NL):
                    dve.wait_ge(lookups, NL * k + (j - RING + 1))
                    make_onehot(j)

            def first_onehots(k, after_lookups=True):
                dve.wait_ge(row_loaded, DMA * (k + 1))
                for n, (j0, j1) in enumerate(ALIKE):
                    inst = nc.vector.tensor_scalar(row_sb[:, j0:j1, :], row_sb[:, j0:j1, :],
                                                   first_rows_sb[:, n:n + 1], None, ALU.subtract)
                inst.then_inc(rows_shifted, 1)
                dve.wait_ge(rows_shifted, k + 1)
                if after_lookups:
                    dve.wait_ge(lookups, NL * k)
                for j in range(RING):
                    make_onehot(j)

            def next_onehot(k, j):
                dve.wait_ge(lookups, NL * k + (j - RING + 1))
                make_onehot(j)

            def wait_dots(k, h):
                dve.wait_ge(dotted, 2 * k + (h + 1))

            def move_quad(k, h, s):
                for n, step in enumerate(LAYOUT):
                    inst = move_dots(nc.vector.tensor_copy, h, s, step)
                    if n < UNDER:
                        inst.then_inc(under_dve, 1)
                        dve.wait_ge(under_dve, UNDER * (4 * k + (2 * h + s)) + (n + 1))
                    elif s == 1:
                        inst.then_inc(pairs_dve, 1)

            def move_half(half):
                before = UNDER * (4 * LAST + 2 + 2 * half)
                for n, step in enumerate(LAYOUT):
                    for s in range(2):
                        if n > 0:
                            dve.wait_ge(under_dve, before + 2 * (n - 1) + s + 1)
                        inst = move_dots(nc.vector.tensor_copy, 1, s, step, half * QT // 2, (half + 1) * QT // 2)
                        if n < UNDER:
                            inst.then_inc(under_dve, 1)
                if half == 1:
                    inst.then_inc(pairs_dve, 1)

            def move_results(k, y=y_ps):
                dve.wait_ge(y_out, k + 1)
                nc.vector.tensor_copy(y_sb[:, bass.ds(2 * k, 2)], y).then_inc(y_moved, 1)

            def dots_and_onehots(k):
                wait_dots(k, 1)
                next_rows(k, 1)
                move_quad(k, 1, 0)
                next_onehot(k + 1, RING + 2)
                next_onehot(k + 1, RING + 3)
                move_quad(k, 1, 1)

            for j in range(RING):
                split_low(j)
            dve.wait_ge(first_rows_loaded, DMA)
            first_onehots(0, False)
            for j in range(RING, NL):
                split_low(j)
                dve.wait_ge(lookups, j - RING + 1)
                make_onehot(j)
            next_rows(0, 0)
            first_onehots(1)
            wait_dots(0, 0)
            move_quad(0, 0, 0)
            move_quad(0, 0, 1)
            next_onehot(1, RING)
            next_onehot(1, RING + 1)
            dots_and_onehots(0)
            with dve.Fori(1, LAST) as k:
                other_onehots(k)
                next_rows(k, 0)
                first_onehots(k + 1)
                wait_dots(k, 0)
                move_quad(k, 0, 0)
                move_quad(k, 0, 1)
                next_onehot(k + 1, RING)
                move_results(k - 1)
                next_onehot(k + 1, RING + 1)
                dots_and_onehots(k)
            other_onehots(LAST)
            wait_dots(LAST, 0)
            move_quad(LAST, 0, 0)
            move_quad(LAST, 0, 1)
            move_results(LAST - 1, last_y_ps)
            dve.wait_ge(half_dotted, 1)
            move_half(0)
            wait_dots(LAST, 1)
            move_half(1)
            move_results(LAST, last_y_ps)

        @block.scalar
        def _(act):
            act.dma_start(counts_sb[:], row_counts).then_inc(ids_loaded, DMA)
            act.dma_start(lookup_counts_sb[:], lookup_counts).then_inc(lookup_ids_loaded, DMA)
            act.dma_start(first_rows_sb[:], first_rows).then_inc(first_rows_loaded, DMA)
            act.dma_start(eye_sb[:], eye).then_inc(eye_loaded, DMA)
            act.sem_inc(pairs_act)
            act.sem_inc(trans_free, 2)
            act.sem_inc(looked_free, 2)

            def round_high(j):
                act.wait_ge(raw_loaded[j % RAW], 2 * DMA * (j // RAW + 1))
                nc.scalar.copy(high[0:RP, CHUNK_AT[j] * P:CHUNK_AT[j + 1] * P],
                               raw[:, j % RAW, 0:CHUNKS[j] * P]).then_inc(high_done, 1)

            round_high(0)
            act.wait_ge(lookup_step, 3)
            act.dma_start(lookup_rows.rearrange("k (j b) -> (k j) b", j=NL), lookup_row[:]).then_inc(lookup_stored, DMA)
            round_high(1)
            round_high(2)
            act.wait_ge(lookup_stored, DMA)
            act.dma_start(row_sb[:], lookup_rows[0:1, :].broadcast_to([P, NL * BS]).rearrange(
                "p (j b) -> p j b", j=NL)).then_inc(row_loaded, DMA)
            round_high(3)

            def move_turned(k, h, g):
                act.wait_ge(turned, 2 * GROUPS * k + (GROUPS * h + g + 1))
                places = group(g)
                nc.scalar.copy(
                    embT[:, h * P:(h + 1) * P, places[0]:places[-1] + 1].rearrange("p b f -> p f b"),
                    trans[g % 2][:, 0:len(places), :]).then_inc(trans_free, 1)

            def move_looked(k, j):
                act.wait_ge(lookups, NL * k + (j + 1))
                nc.scalar.copy(embT[:, :, NG + j - 1:NG + j + 1].rearrange("p b f -> p f b"),
                               looked[j // 2 % 2][:]).then_inc(looked_free, 1)

            def lookups_and_turns(k, with_highs=False):
                for j in range(NL):
                    if with_highs and j + RING + 1 < NL:
                        round_high(j + RING + 1)
                    if j % 2 == 1 and (with_highs or j > 1):
                        move_looked(k, j)
                    for g in turns_after_lookup(j):
                        move_turned(k, 0, g)

            def relu(rnd, u, cols=slice(0, BS)):
                c, (dst, bias) = (u, (h1T, b1_sb)) if u < C1 else (u - C1, (h2T, b2_sb))
                act.wait_ge(layer_out, (C1 + C2) * rnd + (u + 1))
                nc.scalar.activation(dst[:, c, cols], hidden[u % 2][:, cols], ACT.Relu,
                                     bias=bias[:, c:c + 1]).then_inc(relu_done, 1)

            def wait_dots(k, h):
                act.wait_ge(dotted, 2 * k + (h + 1))

            def move_quad(k, h, s):
                for n, step in enumerate(LAYOUT):
                    inst = move_dots(nc.scalar.copy, h, s, step)
                    if n < UNDER:
                        inst.then_inc(under_act, 1)
                        act.wait_ge(under_act, UNDER * (4 * k + (2 * h + s - 2)) + (n + 1))
                    elif s == 3:
                        inst.then_inc(pairs_act, 1)

            def move_half(half):
                before = UNDER * (4 * LAST + 2 + 2 * half)
                for n, step in enumerate(LAYOUT):
                    for s in range(2, 4):
                        if n > 0:
                            act.wait_ge(under_act, before + 2 * (n - 1) + s - 1)
                        inst = move_dots(nc.scalar.copy, 1, s, step, half * QT // 2, (half + 1) * QT // 2)
                        if n < UNDER:
                            inst.then_inc(under_act, 1)
                if half == 1:
                    inst.then_inc(pairs_act, 1)

            def layers_and_turns(k):
                for c in range(C1):
                    relu(k - 1, c)
                    for h, g in turns_after_chunk(c):
                        move_turned(k, h, g)
                wait_dots(k, 0)
                move_quad(k, 0, 2)
                move_quad(k, 0, 3)
                move_turned(k, 1, SECOND_TURNS)
                relu(k - 1, C1)
                move_turned(k, 1, SECOND_TURNS + 1)
                relu(k - 1, C1 + 1)
                move_turned(k, 1, SECOND_TURNS + 2)

            def second_dots(k):
                wait_dots(k, 1)
                move_looked(k + 1, 1)
                move_quad(k, 1, 2)
                move_quad(k, 1, 3)

            lookups_and_turns(0, True)
            for g in range(FIRST_TURNS, GROUPS):
                move_turned(0, 0, g)
            wait_dots(0, 0)
            move_quad(0, 0, 2)
            move_quad(0, 0, 3)
            for g in range(GROUPS):
                move_turned(0, 1, g)
            second_dots(0)
            act.wait_ge(weights_loaded, 5 * DMA)
            with act.Fori(1, LAST) as k:
                lookups_and_turns(k)
                layers_and_turns(k)
                move_turned(k, 1, SECOND_TURNS + 3)
                second_dots(k)
            lookups_and_turns(LAST)
            layers_and_turns(LAST)
            relu(LAST, 0, FIRST_TILE)
            move_turned(LAST, 1, SECOND_TURNS + 3)
            relu(LAST, 1, FIRST_TILE)
            act.wait_ge(half_dotted, 1)
            move_half(0)
            wait_dots(LAST, 1)
            move_half(1)
            for u in range(2, C1 + C2):
                relu(LAST, u, FIRST_TILE)
            for u in range(C1 + C2):
                relu(BLOCKS, u, SECOND_TILE)

        @block.tensor
        def _(pe):
            pe.wait_ge(eye_loaded, DMA)

            def look_up(k, j):
                bank, half = j // 2 % 2, j % 2
                if half == 0:
                    pe.wait_ge(looked_free, LOOKED_BANKS * k + (j // 2 + 1 + (LOOKED_BANKS % 2 if j == 0 else 0)))
                pe.wait_ge(onehot_ready, NL * k + (j + 1))
                for c in range(CHUNKS[j]):
                    at = (CHUNK_AT[j] + c) * P
                    for part in (high, low):
                        inst = nc.tensor.matmul(looked[bank][:, half, :], part[0:RP, at:at + P],
                                                onehot[0:RP, SLOT_AT[j % RING] + c, :],
                                                start=(c == 0 and part is high),
                                                stop=(c == CHUNKS[j] - 1 and part is low))
                inst.then_inc(lookups, 1)

            def turn(k, h, g):
                pe.wait_ge(got[h][g], len(group(g)) * DMA * (k + 1))
                pe.wait_ge(trans_free, 2 * GROUPS * k + (GROUPS * h + g + 1))
                for j, place in enumerate(group(g)):
                    inst = nc.tensor.transpose(trans[g % 2][:, j, :], gathered[:, h, place, :], eye_sb[:])
                inst.then_inc(turned, 1)

            def dot(k, h, halves=False):
                pe.wait_ge(looked_free, LOOKED_BANKS * k + (LOOKED_BANKS + 2))
                pe.wait_ge(trans_free, 2 * GROUPS * k + (GROUPS * (h + 1) + 2))
                pe.wait_ge(pairs_dve, 2 * k + (h + 1))
                pe.wait_ge(pairs_act, 2 * k + (h + 1))
                for t in range(QT):
                    for s in range(QUADS):
                        e = embT[:, h * P + s * QT + t, :]
                        inst = nc.tensor.matmul(dots[32 * s:32 * s + 32, t, :], e, e, start=True, stop=True)
                    if halves and t == QT // 2 - 1:
                        inst.then_inc(half_dotted, 1)
                inst.then_inc(dotted, 1)

            def layer1(rnd, c, cols=slice(0, BS), after_layer3=True):
                if c >= 2 or not after_layer3:
                    pe.wait_ge(relu_done, (C1 + C2) * rnd + (c - 1))
                for r in range(PLANES):
                    inst = nc.tensor.matmul(hidden[c % 2][:, cols], w1_sb[:, r, c * P:(c + 1) * P],
                                            pairs[:, r, cols], start=(r == 0), stop=(r == PLANES - 1))
                inst.then_inc(layer_out, 1)

            def layer2(rnd, c, cols=slice(0, BS)):
                for r in range(C1):
                    if r == 0 or (c == 0 and r == C1 - 1):
                        pe.wait_ge(relu_done, (C1 + C2) * rnd + (C1 if c > 0 or r > 0 else C1 - 1))
                    inst = nc.tensor.matmul(hidden[c % 2][:, cols], w2_sb[:, r, c * P:(c + 1) * P],
                                            h1T[:, r, cols], start=(r == 0), stop=(r == C1 - 1))
                inst.then_inc(layer_out, 1)

            def layer3(k, rounds, y=y_ps):
                pe.wait_ge(relu_done, (C1 + C2) * rounds)
                pe.wait_ge(y_moved, k + 1)
                for h in range(BLOCK_TILES):
                    for r in range(C2):
                        inst = nc.tensor.matmul(y[:, h:h + 1], h2T[:, r, h * P:(h + 1) * P], w3_sb[:, r:r + 1],
                                                start=(r == 0), stop=(r == C2 - 1))
                inst.then_inc(y_out, 1)

            def wait_pairs(tiles, blocks):
                pe.wait_ge(pairs_dve, tiles + 1)
                pe.wait_ge(pairs_act, tiles + 1)
                pe.wait_ge(dense_in, DMA * blocks)

            for j in range(NL):
                pe.wait_ge(low_done, j + 1)
                look_up(0, j)
                for g in turns_after_lookup(j):
                    turn(0, 0, g)
            for g in range(FIRST_TURNS, GROUPS):
                turn(0, 0, g)
            dot(0, 0)
            for g in range(GROUPS):
                if g == GROUPS - 1:
                    look_up(1, 0)
                turn(0, 1, g)
            look_up(1, 1)
            dot(0, 1)
            pe.wait_ge(weights_loaded, 5 * DMA)

            def main_part(k):
                for j in range(1, NL):
                    if j > 1:
                        look_up(k, j)
                    for g in turns_after_lookup(j):
                        turn(k, 0, g)
                wait_pairs(2 * k, k)
                for c in range(C1):
                    layer1(k - 1, c)
                    for h, g in turns_after_chunk(c):
                        turn(k, h, g)
                dot(k, 0)
                turn(k, 1, SECOND_TURNS)
                layer2(k - 1, 0)
                turn(k, 1, SECOND_TURNS + 1)
                layer2(k - 1, 1)

            with pe.Fori(1, LAST) as k:
                main_part(k)
                look_up(k + 1, 0)
                turn(k, 1, SECOND_TURNS + 2)
                layer3(k - 1, k)
                turn(k, 1, SECOND_TURNS + 3)
                look_up(k + 1, 1)
                dot(k, 1)
            main_part(LAST)
            turn(LAST, 1, SECOND_TURNS + 2)
            wait_pairs(TILES - 1, BLOCKS)
            layer1(LAST, 0, FIRST_TILE, False)
            layer3(LAST - 1, LAST, last_y_ps)
            turn(LAST, 1, SECOND_TURNS + 3)
            layer1(LAST, 1, FIRST_TILE, False)
            dot(LAST, 1, True)
            for c in range(2, C1):
                layer1(LAST, c, FIRST_TILE)
            for c in range(C2):
                layer2(LAST, c, FIRST_TILE)
            wait_pairs(TILES, BLOCKS)
            for c in range(C1):
                layer1(BLOCKS, c, SECOND_TILE, False)
            for c in range(C2):
                layer2(BLOCKS, c, SECOND_TILE)
            layer3(LAST, BLOCKS + 1, last_y_ps)


def pair_rows():
    import numpy as np
    lies = {}
    for step in LAYOUT:
        for c, n, m, cols in step:
            for row in range(n):
                for r in range(cols):
                    lies[32 * c + row, r] = (row, m + r)
    where = {f: n for n, f in enumerate(ORDER)}
    first = {}
    for at, pair in lies.items():
        first.setdefault(frozenset(pair), at)
    place = np.full((P, PLANES), -1)
    at = 0
    for a in range(FEATS):
        for b in range(a + 1, FEATS):
            place[first[frozenset((where[a], where[b]))]] = at
            at += 1
    for i in range(DENSE):
        place[96 + DENSE_ROW + i // DENSE_PLANES, DENSE_PLANE + i % DENSE_PLANES] = at + i
    return place


def kernel(**inputs):
    import concourse.bacc as bacc
    import numpy as np
    from concourse.bass_utils import run_bass_kernel_spmd

    tables = [np.ascontiguousarray(inputs[f"tbl_{f}"]) for f in range(FEATS)]
    w_top1 = np.asarray(inputs["W_top1"])
    assert all(tables[f].shape[0] == n for f, n in zip(LOOKED, LOOKED_ROWS))
    counts = np.array([t.shape[0] for t in tables], np.float32)
    arrays = {
        "ids": np.ascontiguousarray(inputs["ids"]),
        "lookup_ids": np.ascontiguousarray(
            np.asarray(inputs["ids"])[:, LOOKED].reshape(P, BLOCKS, BLOCK_TILES, NL).transpose(1, 3, 2, 0)
        ).reshape(BLOCKS * NL, BS),
        "lookup_counts": np.tile(np.stack([counts, counts - 1], 1)[list(LOOKED)], (BLOCKS, 1)),
        "first_rows": np.arange(P, dtype=np.float32)[:, None] * np.array([CHUNKS[j] for j, _ in ALIKE], np.float32),
        "row_counts": np.ascontiguousarray(np.broadcast_to(np.stack([counts, counts - 1]), (P, 2, FEATS))),
        "dense": np.ascontiguousarray(np.pad(
            np.asarray(inputs["dense_ctx"]).reshape(P, BLOCKS, BLOCK_TILES, DENSE).transpose(1, 3, 2, 0),
            ((0, 0), (0, (32 - DENSE_ROW) * DENSE_PLANES - DENSE), (0, 0), (0, 0)))
        ).reshape(BLOCKS, 32 - DENSE_ROW, DENSE_PLANES, BS),
        "eye": np.eye(P, dtype=np.float32),
        "w1": np.ascontiguousarray(np.pad(w_top1, ((0, 1), (0, 0)))[pair_rows()]),
        "b1": np.ascontiguousarray(np.asarray(inputs["b_top1"]).reshape(C1, P).T),
        "w2": np.ascontiguousarray(np.asarray(inputs["W_top2"]).reshape(C1, P, H2).transpose(1, 0, 2)),
        "b2": np.ascontiguousarray(np.asarray(inputs["b_top2"]).reshape(C2, P).T),
        "w3": np.ascontiguousarray(np.asarray(inputs["W_top3"]).reshape(C2, P).T),
    }
    for f, table in enumerate(tables):
        arrays[f"tbl_{f}"] = table

    nc = bacc.Bacc("TRN2", target_bir_lowering=False, num_devices=1)
    ap = {n: nc.dram_tensor(n, a.shape, mybir.dt.from_np(a.dtype), kind="ExternalInput").ap()
          for n, a in arrays.items()}
    out = nc.dram_tensor("y", (BATCH, 1), F32, kind="ExternalOutput").ap()
    build(nc, ap["ids"], ap["lookup_ids"], ap["lookup_counts"], ap["row_counts"], ap["first_rows"],
          [ap[f"tbl_{f}"] for f in range(FEATS)], ap["dense"], ap["eye"],
          ap["w1"], ap["b1"], ap["w2"], ap["b2"], ap["w3"], out)
    return run_bass_kernel_spmd(nc, [arrays], core_ids=[0]).results[0]["y"]
```
